# Optimizing a Trainium2 kernel written in Bass

```python
import numpy as np
import jax
import jax.numpy as jnp

def _softmax(x, axis=-1):
    return jax.nn.softmax(x, axis=axis)

def _gelu(x):
    return jax.nn.gelu(x, approximate=True)

def _silu(x):
    return jax.nn.silu(x)

def _sigmoid(x):
    return jax.nn.sigmoid(x)

def _layernorm(x, axis=-1, eps=1e-05):
    m = jnp.mean(x, axis=axis, keepdims=True)
    v = jnp.var(x, axis=axis, keepdims=True)
    return (x - m) / jnp.sqrt(v + eps)

def _scatter_add(tgt, idx, src, axis=0):
    return tgt.at[idx].add(src)

def _segment_sum(src, seg, n):
    return jax.ops.segment_sum(src, seg, n)
kernel_name = 'mk_dlrm_tower_d1_rec_r8_5a50c4'

def setup_inputs(seed: int=0):
    np.random.seed(seed)
    _w = jnp.asarray

    def _rec_inputs():
        import jax
        import jax.numpy as jnp
        _tk = jax.random.key(seed)
        ids = jnp.stack([jax.random.randint(jax.random.fold_in(_tk, 200 + f), (2048,), 0, v, jnp.int32) for f, v in enumerate([1000, 12500, 12500, 1000, 1250, 125000, 12500, 1000, 1250, 1000, 12500, 1000, 1250, 1250, 1250, 1250, 12500, 1000, 1250, 12500, 12500, 1250, 1000, 1250, 12500, 1000])], axis=1)
        tbl_0 = 0.05 * jax.random.normal(jax.random.fold_in(_tk, 500 + 0), (1000, 128), jnp.float32)
        tbl_1 = 0.05 * jax.random.normal(jax.random.fold_in(_tk, 500 + 1), (12500, 128), jnp.float32)
        tbl_2 = 0.05 * jax.random.normal(jax.random.fold_in(_tk, 500 + 2), (12500, 128), jnp.float32)
        tbl_3 = 0.05 * jax.random.normal(jax.random.fold_in(_tk, 500 + 3), (1000, 128), jnp.float32)
        tbl_4 = 0.05 * jax.random.normal(jax.random.fold_in(_tk, 500 + 4), (1250, 128), jnp.float32)
        tbl_5 = 0.05 * jax.random.normal(jax.random.fold_in(_tk, 500 + 5), (125000, 128), jnp.float32)
        tbl_6 = 0.05 * jax.random.normal(jax.random.fold_in(_tk, 500 + 6), (12500, 128), jnp.float32)
        tbl_7 = 0.05 * jax.random.normal(jax.random.fold_in(_tk, 500 + 7), (1000, 128), jnp.float32)
        tbl_8 = 0.05 * jax.random.normal(jax.random.fold_in(_tk, 500 + 8), (1250, 128), jnp.float32)
        tbl_9 = 0.05 * jax.random.normal(jax.random.fold_in(_tk, 500 + 9), (1000, 128), jnp.float32)
        tbl_10 = 0.05 * jax.random.normal(jax.random.fold_in(_tk, 500 + 10), (12500, 128), jnp.float32)
        tbl_11 = 0.05 * jax.random.normal(jax.random.fold_in(_tk, 500 + 11), (1000, 128), jnp.float32)
        tbl_12 = 0.05 * jax.random.normal(jax.random.fold_in(_tk, 500 + 12), (1250, 128), jnp.float32)
        tbl_13 = 0.05 * jax.random.normal(jax.random.fold_in(_tk, 500 + 13), (1250, 128), jnp.float32)
        tbl_14 = 0.05 * jax.random.normal(jax.random.fold_in(_tk, 500 + 14), (1250, 128), jnp.float32)
        tbl_15 = 0.05 * jax.random.normal(jax.random.fold_in(_tk, 500 + 15), (1250, 128), jnp.float32)
        tbl_16 = 0.05 * jax.random.normal(jax.random.fold_in(_tk, 500 + 16), (12500, 128), jnp.float32)
        tbl_17 = 0.05 * jax.random.normal(jax.random.fold_in(_tk, 500 + 17), (1000, 128), jnp.float32)
        tbl_18 = 0.05 * jax.random.normal(jax.random.fold_in(_tk, 500 + 18), (1250, 128), jnp.float32)
        tbl_19 = 0.05 * jax.random.normal(jax.random.fold_in(_tk, 500 + 19), (12500, 128), jnp.float32)
        tbl_20 = 0.05 * jax.random.normal(jax.random.fold_in(_tk, 500 + 20), (12500, 128), jnp.float32)
        tbl_21 = 0.05 * jax.random.normal(jax.random.fold_in(_tk, 500 + 21), (1250, 128), jnp.float32)
        tbl_22 = 0.05 * jax.random.normal(jax.random.fold_in(_tk, 500 + 22), (1000, 128), jnp.float32)
        tbl_23 = 0.05 * jax.random.normal(jax.random.fold_in(_tk, 500 + 23), (1250, 128), jnp.float32)
        tbl_24 = 0.05 * jax.random.normal(jax.random.fold_in(_tk, 500 + 24), (12500, 128), jnp.float32)
        tbl_25 = 0.05 * jax.random.normal(jax.random.fold_in(_tk, 500 + 25), (1000, 128), jnp.float32)
        _rk = jax.random.fold_in(_tk, 7)
        r_dense_features = -0.000520686 + 1.00062 * jax.random.normal(jax.random.fold_in(_rk, 101), (2048, 128), jnp.float32)
        W_top1 = 0.0405887 * jax.random.normal(jax.random.fold_in(_tk, 801), (607, 512), jnp.float32)
        W_top2 = 0.0441942 * jax.random.normal(jax.random.fold_in(_tk, 802), (512, 256), jnp.float32)
        W_top3 = 0.0625 * jax.random.normal(jax.random.fold_in(_tk, 803), (256, 1), jnp.float32)
        b_top1 = jnp.zeros((512,), jnp.float32)
        b_top2 = jnp.zeros((256,), jnp.float32)
        return (r_dense_features, ids, tbl_0, tbl_1, tbl_2, tbl_3, tbl_4, tbl_5, tbl_6, tbl_7, tbl_8, tbl_9, tbl_10, tbl_11, tbl_12, tbl_13, tbl_14, tbl_15, tbl_16, tbl_17, tbl_18, tbl_19, tbl_20, tbl_21, tbl_22, tbl_23, tbl_24, tbl_25, W_top1, b_top1, W_top2, b_top2, W_top3)
    r_dense_features, ids, tbl_0, tbl_1, tbl_2, tbl_3, tbl_4, tbl_5, tbl_6, tbl_7, tbl_8, tbl_9, tbl_10, tbl_11, tbl_12, tbl_13, tbl_14, tbl_15, tbl_16, tbl_17, tbl_18, tbl_19, tbl_20, tbl_21, tbl_22, tbl_23, tbl_24, tbl_25, W_top1, b_top1, W_top2, b_top2, W_top3 = _rec_inputs()

    def _L0_rec_setup():
        import jax, jax.numpy as jnp
        import numpy as np
        F = 26
        N = F + 1
        _TRIU_I, _TRIU_J = np.triu_indices(N, k=1)
        key = jax.random.key(seed)
        k1, k2 = jax.random.split(key)
        B, D = (2048, 128)
        dense_features = jax.random.normal(k1, (B, D), dtype=jnp.float32)
        sparse_features = jax.random.normal(k2, (B, F, D), dtype=jnp.float32)
        return {'dense_features': dense_features, 'sparse_features': sparse_features}
    _L0_rec_all = _L0_rec_setup()
    _L0_rec_in = {k: v for k, v in _L0_rec_all.items() if k in ()}
    del _L0_rec_all
    return {'r_dense_features': r_dense_features, 'ids': ids, 'tbl_0': tbl_0, 'tbl_1': tbl_1, 'tbl_2': tbl_2, 'tbl_3': tbl_3, 'tbl_4': tbl_4, 'tbl_5': tbl_5, 'tbl_6': tbl_6, 'tbl_7': tbl_7, 'tbl_8': tbl_8, 'tbl_9': tbl_9, 'tbl_10': tbl_10, 'tbl_11': tbl_11, 'tbl_12': tbl_12, 'tbl_13': tbl_13, 'tbl_14': tbl_14, 'tbl_15': tbl_15, 'tbl_16': tbl_16, 'tbl_17': tbl_17, 'tbl_18': tbl_18, 'tbl_19': tbl_19, 'tbl_20': tbl_20, 'tbl_21': tbl_21, 'tbl_22': tbl_22, 'tbl_23': tbl_23, 'tbl_24': tbl_24, 'tbl_25': tbl_25, 'W_top1': W_top1, 'b_top1': b_top1, 'W_top2': W_top2, 'b_top2': b_top2, 'W_top3': W_top3}

def reference(r_dense_features, ids, tbl_0, tbl_1, tbl_2, tbl_3, tbl_4, tbl_5, tbl_6, tbl_7, tbl_8, tbl_9, tbl_10, tbl_11, tbl_12, tbl_13, tbl_14, tbl_15, tbl_16, tbl_17, tbl_18, tbl_19, tbl_20, tbl_21, tbl_22, tbl_23, tbl_24, tbl_25, W_top1, b_top1, W_top2, b_top2, W_top3):
    import jax
    import jax.numpy as jnp

    def _L0_rec_ref(dense_features, sparse_features):
        import jax, jax.numpy as jnp
        import numpy as np
        F = 26
        N = F + 1
        _TRIU_I, _TRIU_J = np.triu_indices(N, k=1)
        combined = jnp.concatenate([dense_features[:, None, :], sparse_features], axis=1)
        interactions = jnp.einsum('bnd,bmd->bnm', combined, combined)
        interactions_flat = interactions[:, _TRIU_I, _TRIU_J]
        return jnp.concatenate([dense_features, interactions_flat], axis=1)
    e = jnp.stack([tbl_0[ids[:, 0]], tbl_1[ids[:, 1]], tbl_2[ids[:, 2]], tbl_3[ids[:, 3]], tbl_4[ids[:, 4]], tbl_5[ids[:, 5]], tbl_6[ids[:, 6]], tbl_7[ids[:, 7]], tbl_8[ids[:, 8]], tbl_9[ids[:, 9]], tbl_10[ids[:, 10]], tbl_11[ids[:, 11]], tbl_12[ids[:, 12]], tbl_13[ids[:, 13]], tbl_14[ids[:, 14]], tbl_15[ids[:, 15]], tbl_16[ids[:, 16]], tbl_17[ids[:, 17]], tbl_18[ids[:, 18]], tbl_19[ids[:, 19]], tbl_20[ids[:, 20]], tbl_21[ids[:, 21]], tbl_22[ids[:, 22]], tbl_23[ids[:, 23]], tbl_24[ids[:, 24]], tbl_25[ids[:, 25]]], axis=1)
    z = _L0_rec_ref(r_dense_features, e)
    z = z.reshape(z.shape[0], -1)
    h = jnp.concatenate([z, r_dense_features], axis=1)
    h = jnp.maximum(h @ W_top1 + b_top1, 0.0)
    h = jnp.maximum(h @ W_top2 + b_top2, 0.0)
    y = h @ W_top3
    return y

_drawn_inputs = setup_inputs


def setup_inputs(seed=0):
    import zlib

    import numpy as np

    out = dict(_drawn_inputs(seed))
    spreads = {'b_top1': (0.0, 0.1), 'b_top2': (0.0, 0.1)}
    factors = {}
    for name, (base, spread) in spreads.items():
        noise = np.random.default_rng([zlib.crc32(name.encode()), seed]).standard_normal(out[name].shape)
        drawn = base * np.exp(spread * noise) if base else spread * noise
        out[name] = jnp.asarray(drawn.astype(out[name].dtype))
    for name, factor in factors.items():
        out[name] = (out[name] * factor).astype(out[name].dtype)
    return out
```

```python
from contextlib import ExitStack

import numpy as np

import concourse.bass as bass
from concourse import mybir

P = 128
TILES = 4
BLK = TILES * P
TABLES = 26
PICKED = [0, 3, 7, 9, 11, 17, 22]
GATHERED = [f for f in range(TABLES) if f not in PICKED]
NPICK = len(PICKED)
NG = len(GATHERED)
NF = TABLES + 1
DENSE = NG
PAIRS = NF * (NF - 1) // 2
PT = 3
PW = PAIRS // PT
ROWS = 1000
RT = 8
RW = ROWS // RT
RING = 2
STAGE = 3
WIDE = 2
GROUPS = P // 4
NW = 32

ALU = mybir.AluOpType
ACT = mybir.ActivationFunctionType
F32 = mybir.dt.float32
F32R = mybir.dt.float32r
I32 = mybir.dt.int32


def place_of_feature():
    return [1 + f for f in GATHERED] + [0] + [1 + f for f in PICKED]


def pair_rows():
    feature = place_of_feature()
    rows = []
    for j in range(1, NF):
        for i in range(j):
            a, b = sorted((feature[i], feature[j]))
            rows.append(P + a * NF - a * (a + 1) // 2 + b - a - 1)
    return np.array(rows)


def build(nc, tables, ids_g, ids_p, dense, consts, w_pairs, w_dense, b1, w2, b2, w3, y):
    NB = dense.shape[0] // BLK
    H1, H2 = w2.shape
    O1, O2 = H1 // P, H2 // P

    FOURS = [list(range(a, min(a + 4, DENSE + 1))) for a in range(0, DENSE + 1, 4)]
    T_TILE = len(FOURS)
    T_BACK = NPICK + TILES * T_TILE
    T_USES = T_BACK + PT
    G_TILE = GROUPS // 8
    TURNS = [[list(range(a, a + 4)), list(range(a + 4, min(a + 7, NF)))] for a in range(1, NF, 7)]
    G_TURN = TILES * G_TILE
    G_USES = G_TURN + len(TURNS)
    M_USES = O1 + O2 + 1
    HOTS = NPICK * RT
    assert T_USES % 2 == 0 and G_USES % 2 == 0

    def on(s, n):
        return (n + 1 - s) // 2

    def T_sent(s, n):
        return on(s, n) - on(s, NPICK)

    def loads(w):
        return len(range(w, NPICK, WIDE))

    with ExitStack() as ctx:
        def sb(name, shape, dt=F32):
            return ctx.enter_context(nc.sbuf_tensor(name, shape, dt))

        def psum(name, shape):
            return ctx.enter_context(nc.psum_tensor(name, shape, F32))

        def sem(name):
            return ctx.enter_context(nc.semaphore(name))

        rows = [sb(f"rows{t}", [P, DENSE + 1, P]) for t in range(TILES)]
        emb = sb("emb", [P, TILES, P * NW])
        emb_f = emb[:, :, :].rearrange("d t (s f) -> d f t s", f=NW)
        emb_q = emb[:, :, :].rearrange("d t (g q f) -> d f q t g", q=4, f=NW)
        hi = [sb(f"hi{f}", [RW, RT, P], F32R) for f in range(NPICK)]
        lo = [sb(f"lo{f}", [RW, RT, P], F32R) for f in range(NPICK)]
        onehot = sb("onehot", [RW, RING, BLK], F32R)
        ids_wide = sb("ids_wide", [RW, WIDE, BLK], I32)
        idx = [sb(f"idx{t}", [P, NG], I32) for t in range(TILES)]
        dots = sb("dots", [P, NF * P])
        dots_j = dots[:, :].rearrange("p (j g) -> p j g", j=NF)
        raw = [dots[0:RW, s * RT * P:(s + 1) * RT * P].rearrange("p (k d) -> p k d", k=RT)
               for s in range(STAGE)]
        h1 = dots[:, 0:O1 * BLK].rearrange("p (o s) -> p o s", o=O1)
        pairs = sb("pairs", [P, 4, PAIRS])
        feats_h2 = sb("feats_h2", [P, PT, BLK])
        feats = feats_h2[0:PW, :, :]
        h2 = feats_h2[:, 0:O2, :]
        y_sb = feats_h2[0:1, PT - 1, :]
        const = sb("const", [P, P + RT])
        ident = const[:, 0:P]
        row_no = const[0:RW, P:P + RT]
        wp = sb("wp", [PW, PT, H1])
        wd = sb("wd", [P, H1])
        wd_second = h2[:, 0, 0:H1]
        w2_sb = sb("w2_sb", [P, O1, H2])
        w3_sb = sb("w3_sb", [P, O2])
        b1_sb = sb("b1_sb", [P, O1])
        b2_sb = sb("b2_sb", [P, O2])

        psT = [psum(f"psT{s}", [P, BLK]) for s in range(2)]
        psG = [psum(f"psG{s}", [P, 8, P]) for s in range(2)]
        psM = [psum(f"psM{s}", [P, BLK]) for s in range(2)]

        const_in = sem("const_in")
        weights_in = sem("weights_in")
        raw_in = [sem(f"raw_in{s}") for s in range(STAGE)]
        hi_done, lo_done = sem("hi_done"), sem("lo_done")
        pad_done = sem("pad_done")
        wd_done = sem("wd_done")
        idx_in = [sem(f"idx_in{t}") for t in range(TILES)]
        wide_in = [sem(f"wide_in{w}") for w in range(WIDE)]
        rows_in = [sem(f"rows_in{t}") for t in range(TILES)]
        dense_in = [sem(f"dense_in{t}") for t in range(TILES)]
        rows_read = [sem(f"rows_read{t}") for t in range(TILES)]
        gather_begun = sem("gather_begun")
        hot_made, hot_free = sem("hot_made"), sem("hot_free")
        T_full = [sem(f"T_full{s}") for s in range(2)]
        T_out = [sem(f"T_out{s}") for s in range(2)]
        G_full = [sem(f"G_full{s}") for s in range(2)]
        G_out_act = [sem(f"G_out_act{s}") for s in range(2)]
        G_out_dve = [sem(f"G_out_dve{s}") for s in range(2)]
        M_full = [sem(f"M_full{s}") for s in range(2)]
        M_out = [sem(f"M_out{s}") for s in range(2)]
        y_out = sem("y_out")

        block = ctx.enter_context(nc.Block())


        def drain_tile(eng, s, i, t, copy):
            for n, four in enumerate(FOURS):
                use = NPICK + t * T_TILE + n
                if use % 2 == s:
                    eng.wait_ge(T_full[s], i * T_sent(s, T_USES) + T_sent(s, use + 1))
                    copy(emb_f[:, four[0]:four[-1] + 1, t, :],
                         psT[s][:, 0:len(four) * P].rearrange("d (f s) -> d f s", s=P)
                         ).then_inc(T_out[s], 1)

        def drain_dots(eng, i, t, samples, G_out, copy):
            for n in range(G_TILE):
                use = t * G_TILE + n
                s = use % 2
                g = t * GROUPS + 8 * n
                eng.wait_ge(G_full[s], i * on(s, G_USES) + on(s, use + 1))
                for q in samples:
                    last = copy(dots_j[32 * q:32 * q + 32, :, g:g + 8].rearrange("p j g -> p g j"),
                                psG[s][32 * q:32 * q + 32, :, q * NF:(q + 1) * NF])
                last.then_inc(G_out[s], 1)

        def drain_pairs(eng, i, half, G_out, copy):
            for n, banks in enumerate(TURNS):
                use = G_TURN + n
                s = use % 2
                eng.wait_ge(G_full[s], i * on(s, G_USES) + on(s, use + 1))
                for k, j in enumerate(banks[half]):
                    at = j * (j - 1) // 2
                    last = copy(pairs[:, :, at:at + j],
                                psG[s][:, 4 * half + k, :].rearrange("g (q i) -> g q i", q=4)[:, :, 0:j])
                last.then_inc(G_out[s], 1)

        def drain_feats(eng, s, i, copy):
            for k in range(PT):
                use = T_BACK + k
                if use % 2 == s:
                    eng.wait_ge(T_full[s], i * T_sent(s, T_USES) + T_sent(s, use + 1))
                    copy(feats[:, k, :], psT[s][0:PW, :]).then_inc(T_out[s], 1)

        def drain_layers(eng, s, i, relu):
            outs = [(h1[:, o, :], b1_sb[:, o:o + 1]) for o in range(O1)]
            outs += [(h2[:, o, :], b2_sb[:, o:o + 1]) for o in range(O2)]
            for use, (out, bias) in enumerate(outs):
                if use % 2 == s:
                    eng.wait_ge(M_full[s], i * on(s, M_USES) + on(s, use + 1))
                    relu(out, psM[s][:, :], bias).then_inc(M_out[s], 1)

        @block.sync
        def _(sp):
            with sp.Fori(0, NB) as i:
                for t in range(TILES):
                    sp.wait_ge(rows_read[t], i + 1)
                    sp.dma_start(idx[t][:, :], ids_g[bass.ds(i * BLK + t * P, P), :]
                                 ).then_inc(idx_in[t], 16)
                    sp.dma_start(rows[t][:, DENSE, :], dense[bass.ds(i * BLK + t * P, P), :]
                                 ).then_inc(dense_in[t], 16)
            sp.wait_ge(y_out, 16 * NB)
            for w in range(WIDE):
                sp.wait_ge(wide_in[w], 16 * (NB * loads(w) + 1))

        @block.gpsimd
        def _(pool):
            with pool.Fori(0, NB) as i:
                for t in range(TILES):
                    pool.wait_ge(idx_in[t], i * 16 + 16)
                    pool.wait_ge(rows_read[t], i + 1)
                    pool.sem_inc(gather_begun, 1)
                    for n in range(NG):
                        pool.indirect_dma_start(
                            rows[t][:, n, :], None, tables[GATHERED[n]],
                            bass.IndirectOffsetOnAxis(idx[t][:, n:n + 1], 0)).then_inc(rows_in[t], 16)

        @block.scalar
        def _(act):
            def copy(out, in_):
                return nc.scalar.copy(out, in_)

            def relu(out, in_, bias):
                return nc.scalar.activation(out, in_, ACT.Relu, bias=bias)

            def load_table(f):
                act.dma_start(raw[f % STAGE], tables[PICKED[f]].rearrange("(k p) d -> p k d", p=RW)
                              ).then_inc(raw_in[f % STAGE], 16)

            def load_wide(i, f):
                act.dma_start(ids_wide[:, f % WIDE, :],
                              ids_p[f:f + 1, bass.ds(i * BLK, BLK)].to_broadcast([RW, BLK])
                              ).then_inc(wide_in[f % WIDE], 16)

            load_table(0)
            act.dma_start(const[:, :], consts).then_inc(const_in, 16)
            for f in range(1, STAGE):
                load_table(f)
            for f in range(WIDE):
                load_wide(0, f)
            for f in range(NPICK):
                act.wait_ge(raw_in[f % STAGE], 16 * (f // STAGE + 1))
                copy(hi[f][:, :, :], raw[f % STAGE]).then_inc(hi_done, 1)
                if f + STAGE < NPICK:
                    act.wait_ge(lo_done, f + 1)
                    load_table(f + STAGE)
            for out, in_ in ((wd[:, :], w_dense[0]), (wd_second, w_dense[1]),
                             (wp[:, :, :], w_pairs.rearrange("(k p) n -> p k n", p=PW)),
                             (w2_sb[:, :, :], w2.rearrange("(k p) n -> p k n", p=P)),
                             (w3_sb[:, :], w3),
                             (b1_sb[:, :], b1), (b2_sb[:, :], b2)):
                act.dma_start(out, in_).then_inc(weights_in, 16)
            act.wait_ge(weights_in, 7 * 16)
            with act.Fori(0, NB) as i:
                for f in range(NPICK):
                    act.wait_ge(hot_free, i * HOTS + (f + 1) * RT + RING)
                    copy(emb_f[:, DENSE + 1 + f, :, :],
                         psT[f % 2][:, :].rearrange("d (t s) -> d t s", t=TILES)
                         ).then_inc(T_out[f % 2], 1)
                    if f + WIDE < NPICK:
                        load_wide(i, f + WIDE)
                    else:
                        load_wide(i + 1, f % WIDE)
                for t in range(TILES):
                    drain_tile(act, 0, i, t, copy)
                    drain_dots(act, i, t, (0, 1), G_out_act, copy)
                drain_pairs(act, i, 0, G_out_act, copy)
                drain_feats(act, 0, i, copy)
                drain_layers(act, 0, i, relu)
                act.wait_ge(M_full[0], i * on(0, M_USES) + on(0, M_USES))
                copy(y_sb[:, :].rearrange("o (t g q) -> o q t g", t=TILES, q=4),
                     psM[0][0:1, :].rearrange("o (q t g) -> o q t g", q=4, t=TILES)
                     ).then_inc(M_out[0], 1)
                act.wait_ge(M_out[0], i * on(0, M_USES) + on(0, M_USES) + 1)
                act.dma_start(y[:, bass.ds(i * BLK, BLK)], y_sb[:, :]).then_inc(y_out, 16)
                act.wait_ge(y_out, i * 16 + 16)

        @block.vector
        def _(dve):
            def copy(out, in_):
                return nc.vector.tensor_copy(out, in_)

            def relu(out, in_, bias):
                return nc.vector.tensor_scalar(out, in_, bias, 0.0, ALU.add, ALU.max)

            nc.vector.memset(emb_f[:, NF:NW, :, :], 0.0).then_inc(pad_done, 1)
            for f in range(NPICK):
                dve.wait_ge(hi_done, f + 1)
                nc.vector.tensor_tensor(lo[f][:, :, :], raw[f % STAGE], hi[f][:, :, :].bitcast(F32),
                                        ALU.subtract).then_inc(lo_done, 1)
            dve.wait_ge(const_in, 16)
            dve.wait_ge(weights_in, 7 * 16)
            nc.vector.tensor_tensor(wd[:, :], wd[:, :], wd_second, ALU.add).then_inc(wd_done, 1)
            with dve.Fori(0, NB) as i:
                for n in range(HOTS):
                    f, k = divmod(n, RT)
                    if k == 0:
                        w = f % WIDE
                        dve.wait_ge(wide_in[w], i * 16 * loads(w) + 16 * (f // WIDE + 1))
                    dve.wait_ge(hot_free, i * HOTS + n + 1)
                    nc.vector.tensor_scalar(onehot[:, n % RING, :], ids_wide[:, f % WIDE, :],
                                            row_no[:, k:k + 1], None, ALU.is_equal
                                            ).then_inc(hot_made, 1)
                for t in range(TILES):
                    drain_tile(dve, 1, i, t, copy)
                    drain_dots(dve, i, t, (2, 3), G_out_dve, copy)
                drain_pairs(dve, i, 1, G_out_dve, copy)
                drain_feats(dve, 1, i, copy)
                drain_layers(dve, 1, i, relu)

        @block.tensor
        def _(pe):
            def T_slot(i, use):
                s = use % 2
                pe.wait_ge(T_out[s], i * on(s, T_USES) + on(s, use) + 1)
                return s

            def G_slot(i, use):
                s = use % 2
                pe.wait_ge(G_out_act[s], i * on(s, G_USES) + on(s, use) + 1)
                pe.wait_ge(G_out_dve[s], i * on(s, G_USES) + on(s, use) + 1)
                return s

            def M_slot(i, use):
                s = use % 2
                pe.wait_ge(M_out[s], i * on(s, M_USES) + on(s, use) + 1)
                return s

            def T_copied(i, n):
                for s in range(2):
                    pe.wait_ge(T_out[s], i * on(s, T_USES) + on(s, n) + 1)

            def G_copied(i, n):
                for s in range(2):
                    pe.wait_ge(G_out_act[s], i * on(s, G_USES) + on(s, n) + 1)
                    pe.wait_ge(G_out_dve[s], i * on(s, G_USES) + on(s, n) + 1)

            pe.sem_inc(hot_free, RING)
            for free in (*T_out, *G_out_act, *G_out_dve, *M_out, *rows_read):
                pe.sem_inc(free, 1)
            pe.wait_ge(const_in, 16)
            pe.wait_ge(pad_done, 1)
            with pe.Fori(0, NB) as i:
                for f in range(NPICK):
                    pe.wait_ge(lo_done, f + 1)
                    s = T_slot(i, f)
                    for k in range(RT):
                        n = f * RT + k
                        pe.wait_ge(hot_made, i * HOTS + n + 1)
                        nc.tensor.matmul(psT[s][:, :], hi[f][:, k, :], onehot[:, n % RING, :],
                                         start=(k == 0), stop=False)
                        nc.tensor.matmul(psT[s][:, :], lo[f][:, k, :], onehot[:, n % RING, :],
                                         start=False, stop=(k == RT - 1)).then_inc(hot_free, 1)
                for t in range(TILES):
                    pe.wait_ge(rows_in[t], i * (16 * NG) + 16 * NG)
                    pe.wait_ge(dense_in[t], i * 16 + 16)
                    for n, four in enumerate(FOURS):
                        s = T_slot(i, NPICK + t * T_TILE + n)
                        for k, f in enumerate(four):
                            last = nc.tensor.transpose(psT[s][:, k * P:(k + 1) * P],
                                                       rows[t][:, f, :], ident)
                        last.then_inc(T_full[s], 1)
                    T_copied(i, NPICK + (t + 1) * T_TILE)
                    pe.sem_inc(rows_read[t], 1)
                    for n in range(G_TILE):
                        s = G_slot(i, t * G_TILE + n)
                        for k in range(8):
                            at = 4 * (8 * n + k) * NW
                            group = emb[:, t, at:at + 4 * NW]
                            last = nc.tensor.matmul(
                                psG[s][:, k, 0:4 * NF], group,
                                group.rearrange("d (q f) -> d q f", q=4)[:, :, 0:NF],
                                start=True, stop=True)
                        last.then_inc(G_full[s], 1)
                G_copied(i, G_TURN)
                for n, banks in enumerate(TURNS):
                    s = G_slot(i, G_TURN + n)
                    for half in range(2):
                        for k, j in enumerate(banks[half]):
                            last = nc.tensor.transpose(psG[s][:, 4 * half + k, :], dots_j[:, j, :], ident)
                    last.then_inc(G_full[s], 1)
                G_copied(i, G_USES)
                for k in range(PT):
                    s = T_slot(i, T_BACK + k)
                    for q in range(4):
                        last = nc.tensor.transpose(psT[s][0:PW, q * P:(q + 1) * P],
                                                   pairs[:, q, k * PW:(k + 1) * PW], ident)
                    last.then_inc(T_full[s], 1)
                pe.wait_ge(weights_in, 7 * 16)
                pe.wait_ge(wd_done, 1)
                T_copied(i, T_USES)
                for o in range(O1):
                    s = M_slot(i, o)
                    for k in range(PT):
                        nc.tensor.matmul(psM[s][:, :], wp[:, k, o * P:(o + 1) * P], feats[:, k, :],
                                         start=(k == 0), stop=False)
                    nc.tensor.matmul(psM[s][:, :], wd[:, o * P:(o + 1) * P], emb_q[:, DENSE],
                                     start=False, stop=True).then_inc(M_full[s], 1)
                for o in range(O2):
                    s = M_slot(i, O1 + o)
                    for k in range(O1):
                        pe.wait_ge(M_out[k % 2], i * on(k % 2, M_USES) + on(k % 2, k + 1) + 1)
                        last = nc.tensor.matmul(psM[s][:, :], w2_sb[:, k, o * P:(o + 1) * P],
                                                h1[:, k, :], start=(k == 0), stop=(k == O1 - 1))
                    last.then_inc(M_full[s], 1)
                s = M_slot(i, O1 + O2)
                for k in range(O2):
                    use = O1 + k
                    pe.wait_ge(M_out[use % 2], i * on(use % 2, M_USES) + on(use % 2, use + 1) + 1)
                    last = nc.tensor.matmul(psM[s][0:1, :], w3_sb[:, k:k + 1], h2[:, k, :],
                                            start=(k == 0), stop=(k == O2 - 1))
                last.then_inc(M_full[s], 1)


def kernel(**inputs):
    import concourse.bacc as bacc
    from concourse.bass_utils import run_bass_kernel_spmd

    ids = np.asarray(inputs["ids"])
    w1 = np.asarray(inputs["W_top1"])
    batch = ids.shape[0]
    arrays = {f"tbl_{f}": np.ascontiguousarray(inputs[f"tbl_{f}"]) for f in range(TABLES)}
    arrays["ids_g"] = np.ascontiguousarray(ids[:, GATHERED])
    arrays["ids_p"] = np.zeros((NPICK, batch + BLK), ids.dtype)
    arrays["ids_p"][:, :batch] = ids[:, PICKED].T
    arrays["dense"] = np.ascontiguousarray(inputs["r_dense_features"])
    consts = np.zeros((P, P + RT), np.float32)
    consts[:, :P] = np.eye(P)
    consts[:, P:] = np.arange(P)[:, None] + RW * np.arange(RT)
    arrays["consts"] = consts
    arrays["w_pairs"] = np.ascontiguousarray(w1[pair_rows()])
    arrays["w_dense"] = np.ascontiguousarray(np.stack([w1[:P], w1[P + PAIRS:]]))
    arrays["b1"] = np.ascontiguousarray(np.asarray(inputs["b_top1"]).reshape(-1, P).T)
    arrays["w2"] = np.ascontiguousarray(inputs["W_top2"])
    arrays["b2"] = np.ascontiguousarray(np.asarray(inputs["b_top2"]).reshape(-1, P).T)
    arrays["w3"] = np.ascontiguousarray(np.asarray(inputs["W_top3"]).reshape(-1, P).T)

    nc = bacc.Bacc("TRN2", target_bir_lowering=False, num_devices=1)
    ap = {n: nc.dram_tensor(n, a.shape, mybir.dt.from_np(a.dtype), kind="ExternalInput").ap()
          for n, a in arrays.items()}
    y = nc.dram_tensor("y", (1, batch), F32, kind="ExternalOutput").ap()
    build(nc, [ap[f"tbl_{f}"] for f in range(TABLES)], ap["ids_g"], ap["ids_p"], ap["dense"],
          ap["consts"], ap["w_pairs"], ap["w_dense"], ap["b1"], ap["w2"], ap["b2"], ap["w3"], y)
    result = run_bass_kernel_spmd(nc, [arrays], core_ids=[0])
    return np.asarray(result.results[0]["y"]).reshape(batch, 1)
```

```python
from contextlib import ExitStack

import numpy as np

import concourse.bass as bass
from concourse import mybir

P = 128
TILES = 4
BLK = TILES * P
TABLES = 26
PICKED = [0, 3, 7, 9, 11, 17, 22]
GATHERED = [f for f in range(TABLES) if f not in PICKED]
NPICK = len(PICKED)
NG = len(GATHERED)
NF = TABLES + 1
DENSE = NG
PAIRS = NF * (NF - 1) // 2
PT = 3
PW = PAIRS // PT
ROWS = 1000
RT = 8
RW = ROWS // RT
KEPT = 4
SOON = NPICK - KEPT
RING = 3
WIDE = 2
GROUPS = P // 4
NW = 32
USED = 4 * NW - (NW - NF + 1)

ALU = mybir.AluOpType
ACT = mybir.ActivationFunctionType
F32 = mybir.dt.float32
F32R = mybir.dt.float32r
I32 = mybir.dt.int32


def place_of_feature():
    return [1 + f for f in GATHERED] + [0] + [1 + f for f in PICKED]


def pair_rows():
    feature = place_of_feature()
    rows = []
    for j in range(1, NF):
        for i in range(j):
            a, b = sorted((feature[i], feature[j]))
            rows.append(P + a * NF - a * (a + 1) // 2 + b - a - 1)
    return np.array(rows)


def build(nc, tables, ids_g, ids_p, dense, consts, w_pairs, w_dense, b1, w2, last, y):
    NB = dense.shape[0] // BLK
    H1, H2 = w2.shape
    O1 = H1 // P

    FOURS = [list(range(a, min(a + 4, DENSE + 1))) for a in range(0, DENSE + 1, 4)]
    LAST = len(FOURS) - 1

    def tile_fills(t):
        return [("tile", t, n) for n in range(len(FOURS))]

    EARLY = [("pick", 0), ("pick", 1), *tile_fills(0), ("pick", 2), *tile_fills(1),
             ("pick", 3), ("pick", 4), *tile_fills(2), ("pick", 5), ("pick", 6), *tile_fills(3)]
    assert SOON == 3 and KEPT == 4
    FILLS = {what: (n % 4, "dve" if what[0] == "tile" and what[2] % 2 else "act")
             for n, what in enumerate(EARLY)}
    a, b, c, d = [(len(EARLY) + n) % 4 for n in range(4)]
    FILLS |= {("back", 0): (c, "act"), ("back", 1): (d, "dve"), ("back", 2): (c, "act"),
              ("one", 0): (a, "dve"), ("one", 1): (b, "act"), ("one", 2): (d, "dve"),
              ("one", 3): (c, "act"), ("two", 0): (a, "dve"), ("two", 1): (b, "dve"),
              ("two", 2): (d, "dve"), ("two", 3): (c, "dve")}
    ORDER = list(FILLS)
    assert PT == 3 and O1 == 4 and 2 * P == H2

    def left_out(i, what):
        return isinstance(i, int) and i == NB - 1 and what[0] == "pick" and what[1] >= SOON

    def before(i, what, signalled=False):
        return sum(FILLS[x][0] == FILLS[what][0] and not (signalled and x[0] == "pick")
                   and not left_out(i, x) for x in ORDER[:ORDER.index(what)])

    def in_block(bank, signalled=False):
        return sum(FILLS[x][0] == bank and not (signalled and x[0] == "pick") for x in ORDER)

    def ahead(i):
        return isinstance(i, int) and i == -1

    def pick_bank(i, pick):
        return pick - SOON if ahead(i) else FILLS["pick", pick][0]

    def out_count(i, what):
        return i * in_block(FILLS[what][0]) + before(i, what) + 2

    G_TILE = GROUPS // 8
    TURNS = [[list(range(a, a + 4)), list(range(a + 4, min(a + 7, NF)))] for a in range(1, NF, 7)]
    G_TURN = TILES * G_TILE
    G_USES = G_TURN + len(TURNS)
    HOTS = NPICK * RT
    assert G_USES % 2 == 0

    def on(s, n):
        return (n + 1 - s) // 2

    AHEAD = KEPT * RT

    def hot_count(i, n):
        return i * HOTS + n + 1 + AHEAD

    def hot_user(n):
        return max([m for m in range(n) if m % RING == n % RING] or
                   [m - HOTS for m in range(HOTS) if m % RING == n % RING])

    def table_of(pick):
        return (pick + KEPT) % NPICK

    def ids_count(i, pick):
        w = pick % WIDE
        a_block = len(range(w, NPICK, WIDE))
        return i * a_block + pick // WIDE + 1 + sum(p % WIDE == w for p in range(SOON, NPICK))

    with ExitStack() as ctx:
        def sb(name, shape, dt=F32):
            return ctx.enter_context(nc.sbuf_tensor(name, shape, dt))

        def psum(name, shape):
            return ctx.enter_context(nc.psum_tensor(name, shape, F32))

        def sem(name):
            return ctx.enter_context(nc.semaphore(name))

        rows = [sb(f"rows{t}", [P, DENSE + 1, P]) for t in range(TILES)]
        emb = sb("emb", [P, TILES, P * NW])
        emb_f = emb[:, :, :].rearrange("d t (s f) -> d f t s", f=NW)
        emb_q = emb[:, :, :].rearrange("d t (g q f) -> d f q t g", q=4, f=NW)
        hi = [sb(f"hi{f}", [RW, RT, P], F32R) for f in range(NPICK)]
        lo = [sb(f"lo{f}", [RW, RT, P], F32R) for f in range(NPICK)]
        onehot = sb("onehot", [RW, RING, BLK], F32R)
        ids_wide = sb("ids_wide", [RW, WIDE, BLK], I32)
        idx = [sb(f"idx{t}", [P, NG], I32) for t in range(TILES)]
        dots = sb("dots", [P, (NF - 1) * P])
        dots_j = dots[:, :].rearrange("p (j g) -> p j g", j=NF - 1)
        raw = [dots[0:RW, s * RT * P:(s + 1) * RT * P].rearrange("p (k d) -> p k d", k=RT)
               for s in range(3)]
        raw += [rows[t][0:RW, a:a + RT, :] for t in (2, 3) for a in (0, RT)]
        h1 = dots[:, 0:O1 * BLK].rearrange("p (o s) -> p o s", o=O1)
        pairs = sb("pairs", [P, 4, PAIRS])
        feats_h2 = sb("feats_h2", [P, PT, BLK])
        feats = feats_h2[0:PW, :, :]
        h2 = feats_h2[:, 0, :].rearrange("p (a n) -> p a n", a=2)
        wd_second = feats_h2[:, 1, 0:H1]
        last_in = feats_h2[:, 2, :]
        b2_row, w3_row = emb_f[:, NF, 0:2, :], emb_f[:, NF + 1, 0:2, :]
        kept = [emb_f[:, NF + 2 + f, :, :].rearrange("d (a b) s -> d a b s", a=2)
                for f in range(KEPT - 1)] + [emb_f[:, NF:NF + 2, 2:TILES, :]]
        assert KEPT == NW - NF - 1 and TILES == 4
        const = sb("const", [P, P + RT])
        ident = const[:, 0:P]
        row_no = const[0:RW, P:P + RT]
        wp = sb("wp", [PW, PT, H1])
        wd = sb("wd", [P, H1])
        w2_sb = sb("w2_sb", [P, O1, H2])
        b1_sb = sb("b1_sb", [P, O1])
        y_sb = sb("y_sb", [P, 4])

        bank = [psum(f"bank{s}", [P, BLK]) for s in range(4)]
        psG = [psum(f"psG{s}", [P, 8, P]) for s in range(2)]

        const_in = sem("const_in")
        weights_in = sem("weights_in")
        raw_in = [sem(f"raw_in{f}") for f in range(NPICK)]
        hi_done, lo_done = sem("hi_done"), sem("lo_done")
        rows_done = sem("rows_done")
        moved = sem("moved")
        wd_done = sem("wd_done")
        idx_in = [sem(f"idx_in{t}") for t in range(TILES)]
        wide_in = [sem(f"wide_in{w}") for w in range(WIDE)]
        rows_in = [sem(f"rows_in{t}") for t in range(TILES)]
        dense_in = [sem(f"dense_in{t}") for t in range(TILES)]
        rows_read = [sem(f"rows_read{t}") for t in range(TILES)]
        gather_begun = sem("gather_begun")
        hot_made, hot_free = sem("hot_made"), sem("hot_free")
        bank_full = [sem(f"bank_full{s}") for s in range(4)]
        bank_out = [sem(f"bank_out{s}") for s in range(4)]
        G_full = [sem(f"G_full{s}") for s in range(2)]
        G_out_act = [sem(f"G_out_act{s}") for s in range(2)]
        G_out_dve = [sem(f"G_out_dve{s}") for s in range(2)]
        h2_sum, h2_done = sem("h2_sum"), sem("h2_done")
        y_out = sem("y_out")

        block = ctx.enter_context(nc.Block())

        def drain(eng, name, i, what, copy, *args):
            s, by = FILLS[what]
            if by == name:
                eng.wait_ge(bank_full[s], i * in_block(s, True) + before(i, what, True) + 1)
                copy(*args).then_inc(bank_out[s], 1)

        def drain_tile(eng, name, i, t, copy):
            for n, four in enumerate(FOURS):
                s = FILLS["tile", t, n][0]
                drain(eng, name, i, ("tile", t, n), copy, emb_f[:, four[0]:four[-1] + 1, t, :],
                      bank[s][:, 0:len(four) * P].rearrange("d (f s) -> d f s", s=P))

        def drain_dots(eng, i, t, part, samples, G_out, copy):
            for n in part:
                use = t * G_TILE + n
                s = use % 2
                g = t * GROUPS + 8 * n
                eng.wait_ge(G_full[s], i * on(s, G_USES) + on(s, use + 1))
                for q in samples:
                    end = min(NW * q + NW, USED)
                    last = copy(dots_j[NW * q:end, :, g:g + 8].rearrange("p j g -> p g j"),
                                psG[s][NW * q:end, :, q * (NF - 1):(q + 1) * (NF - 1)])
                last.then_inc(G_out[s], 1)

        def drain_pairs(eng, i, half, G_out, copy):
            for n, banks in enumerate(TURNS):
                use = G_TURN + n
                s = use % 2
                eng.wait_ge(G_full[s], i * on(s, G_USES) + on(s, use + 1))
                for k, j in enumerate(banks[half]):
                    at = j * (j - 1) // 2
                    last = copy(pairs[:, :, at:at + j],
                                psG[s][:, 4 * half + k, :].rearrange("g (q i) -> g q i", q=4)[:, :, 0:j])
                last.then_inc(G_out[s], 1)

        def drain_feats(eng, name, i, copy):
            for k in range(PT):
                s = FILLS["back", k][0]
                drain(eng, name, i, ("back", k), copy, feats[:, k, :], bank[s][0:PW, :])

        def drain_layers(eng, name, i, relu):
            for o in range(O1):
                s = FILLS["one", o][0]
                drain(eng, name, i, ("one", o), relu, h1[:, o, :], bank[s][:, :], b1_sb[:, o:o + 1])

        FIRST, SECOND = range(G_TILE - 1), range(G_TILE - 1, G_TILE)

        @block.sync
        def _(sp):
            with sp.Fori(0, NB) as i:
                for t in range(TILES):
                    sp.wait_ge(rows_read[t], i + 1)
                    sp.dma_start(idx[t][:, :], ids_g[bass.ds(i * BLK + t * P, P), :]
                                 ).then_inc(idx_in[t], 16)
                    sp.dma_start(rows[t][:, DENSE, :], dense[bass.ds(i * BLK + t * P, P), :]
                                 ).then_inc(dense_in[t], 16)
            sp.wait_ge(y_out, 16 * NB)

        @block.gpsimd
        def _(pool):
            with pool.Fori(0, NB) as i:
                for t in range(TILES):
                    pool.wait_ge(idx_in[t], i * 16 + 16)
                    pool.wait_ge(rows_read[t], i + 1)
                    if t >= 2:
                        pool.wait_ge(lo_done, NPICK)
                    pool.sem_inc(gather_begun, 1)
                    for n in range(NG):
                        pool.indirect_dma_start(
                            rows[t][:, n, :], None, tables[GATHERED[n]],
                            bass.IndirectOffsetOnAxis(idx[t][:, n:n + 1], 0)).then_inc(rows_in[t], 16)

        @block.scalar
        def _(act):
            def copy(out, in_):
                return nc.scalar.copy(out, in_)

            def relu(out, in_, bias):
                return nc.scalar.activation(out, in_, ACT.Relu, bias=bias)

            def load_wide(i, pick):
                f, block = table_of(pick), i + (pick >= SOON)
                act.dma_start(ids_wide[:, pick % WIDE, :],
                              ids_p[f:f + 1, bass.ds(block * BLK, BLK)].to_broadcast([RW, BLK])
                              ).then_inc(wide_in[pick % WIDE], 16)

            def drain_pick(i, pick, last=False):
                n = (pick + 1) * RT - 1
                act.wait_ge(hot_made, hot_count(i, n))
                if pick + WIDE < (SOON if last else NPICK):
                    load_wide(i, pick + WIDE)
                elif not last:
                    load_wide(i + 1, pick % WIDE)
                act.wait_ge(hot_free, hot_count(i, n) + RING)
                s = pick_bank(i, pick)
                if pick < SOON:
                    copy(emb_f[:, DENSE + 1 + table_of(pick), :, :],
                         bank[s][:, :].rearrange("d (t s) -> d t s", t=TILES)
                         ).then_inc(bank_out[s], 1)
                else:
                    copy(kept[pick - SOON], bank[s][:, :].rearrange("d (a b s) -> d a b s", a=2, b=2)
                         ).then_inc(bank_out[s], 1)

            def move_kept(i):
                for pick in range(SOON, NPICK):
                    s = pick_bank(i, pick)
                    act.wait_ge(bank_out[s], 1 if ahead(i) else out_count(i, ("pick", pick)))
                    copy(emb_f[:, DENSE + 1 + table_of(pick), :, :
                               ].rearrange("d (a b) s -> d a b s", a=2),
                         kept[pick - SOON]).then_inc(moved, 1)

            for f in range(NPICK):
                act.dma_start(raw[f], tables[PICKED[f]].rearrange("(k p) d -> p k d", p=RW)
                              ).then_inc(raw_in[f], 16)
                if f < WIDE:
                    load_wide(-1, SOON + f)
                if f == 0:
                    act.dma_start(const[:, :], consts).then_inc(const_in, 16)
            for f in range(NPICK):
                act.wait_ge(raw_in[f], 16)
                copy(hi[f][:, :, :], raw[f]).then_inc(hi_done, 1)
            for out, in_ in ((wd[:, :], w_dense[0]), (wd_second, w_dense[1]),
                             (wp[:, :, :], w_pairs.rearrange("(k p) n -> p k n", p=PW)),
                             (w2_sb[:, :, :], w2.rearrange("(k p) n -> p k n", p=P)),
                             (last_in, last.to_broadcast([P, 2 * H2])), (b1_sb[:, :], b1)):
                act.dma_start(out, in_).then_inc(weights_in, 16)
            for pick in range(SOON, NPICK):
                drain_pick(-1, pick)
            move_kept(-1)

            def work(i, last=False):
                drain_pick(i, 0, last)
                drain_pick(i, 1, last)
                drain_tile(act, "act", i, 0, copy)
                drain_pick(i, 2, last)
                drain_tile(act, "act", i, 1, copy)
                for t in range(TILES):
                    drain_dots(act, i, t, FIRST, (0, 1), G_out_act, copy)
                    if 1 <= t < TILES - 1:
                        if not last:
                            drain_pick(i, 2 * t + 1)
                            drain_pick(i, 2 * t + 2)
                        drain_tile(act, "act", i, t + 1, copy)
                    drain_dots(act, i, t, SECOND, (0, 1), G_out_act, copy)
                drain_pairs(act, i, 0, G_out_act, copy)
                drain_feats(act, "act", i, copy)
                act.wait_ge(weights_in, 6 * 16)
                drain_layers(act, "act", i, relu)
                if not last:
                    move_kept(i)
                act.wait_ge(h2_done, i * 4 + 4)
                act.dma_start(y[:, bass.ds(i * BLK, BLK)].rearrange("o (p q) -> (o p) q", q=4),
                              y_sb[:, :]).then_inc(y_out, 16)
                act.wait_ge(y_out, i * 16 + 16)

            with act.Fori(0, NB - 1) as i:
                work(i)
            work(NB - 1, last=True)

        @block.vector
        def _(dve):
            def add_bias(out, in_):
                return nc.vector.tensor_tensor(out.rearrange("p (t s) -> p t s", t=2),
                                               in_.rearrange("p (t s) -> p t s", t=2), b2_row, ALU.add)

            def copy(out, in_):
                return nc.vector.tensor_copy(out, in_)

            def relu(out, in_, bias):
                return nc.vector.tensor_scalar(out, in_, bias, 0.0, ALU.add, ALU.max)

            def make_lo(f):
                dve.wait_ge(hi_done, f + 1)
                nc.vector.tensor_tensor(lo[f][:, :, :], raw[f], hi[f][:, :, :].bitcast(F32),
                                        ALU.subtract).then_inc(lo_done, 1)

            def make_hots(i, part):
                for n in part:
                    pick, k = divmod(n, RT)
                    if k == 0:
                        dve.wait_ge(wide_in[pick % WIDE], ids_count(i, pick) * 16)
                    dve.wait_ge(hot_free, hot_count(i, hot_user(n)) + RING)
                    nc.vector.tensor_scalar(onehot[:, n % RING, :], ids_wide[:, pick % WIDE, :],
                                            row_no[:, k:k + 1], None, ALU.is_equal
                                            ).then_inc(hot_made, 1)

            def hots_of(first, last):
                return range(first * RT + RING, (last + 1) * RT)

            def first_hots(pick):
                return range(pick * RT, pick * RT + RING)

            def start_block(i):
                make_hots(i, hots_of(0, 1))
                make_hots(i, first_hots(2))
                drain_tile(dve, "dve", i, 0, copy)
                make_hots(i, hots_of(2, 2))

            def work(i, last=False):
                drain_tile(dve, "dve", i, 1, copy)
                for t in range(TILES):
                    if not last:
                        if t == 0:
                            make_hots(i, first_hots(3))
                        if t == 3:
                            make_hots(i + 1, first_hots(0))
                    drain_dots(dve, i, t, FIRST, (2, 3), G_out_dve, copy)
                    if 1 <= t < TILES - 1:
                        if not last:
                            make_hots(i, hots_of(2 * t + 1, 2 * t + 2))
                        drain_tile(dve, "dve", i, t + 1, copy)
                        if t == 1 and not last:
                            make_hots(i, first_hots(5))
                    drain_dots(dve, i, t, SECOND, (2, 3), G_out_dve, copy)
                drain_pairs(dve, i, 1, G_out_dve, copy)
                drain_feats(dve, "dve", i, copy)
                drain_layers(dve, "dve", i, relu)
                for q in range(4):
                    s = FILLS["two", q][0]
                    drain(dve, "dve", i, ("two", q), add_bias, h2[:, q % 2, :],
                          bank[s][:, 0:H2])
                    dve.wait_ge(bank_out[s], out_count(i, ("two", q)))
                    nc.vector.scalar_tensor_tensor(
                        h2[:, q % 2, :].rearrange("p (t s) -> p t s", t=2),
                        h2[:, q % 2, :].rearrange("p (t s) -> p t s", t=2), 0.0, w3_row,
                        ALU.max, ALU.mult, accum_out=y_sb[:, q:q + 1]).then_inc(h2_done, 1)

            make_lo(0)
            dve.wait_ge(const_in, 16)
            for f in range(NPICK - 1):
                make_lo(f + 1)
                i, pick = (-1, SOON + f) if f < KEPT else (0, f - KEPT)
                make_hots(i, range(pick * RT, (pick + 1) * RT))
            dve.wait_ge(weights_in, 6 * 16)
            nc.vector.tensor_tensor(wd[:, :], wd[:, :], wd_second, ALU.add).then_inc(wd_done, 1)
            nc.vector.tensor_copy(b2_row, last_in[:, 0:H2].rearrange("p (t s) -> p t s", t=2)
                                  ).then_inc(rows_done, 1)
            nc.vector.tensor_copy(w3_row, last_in[:, H2:2 * H2].rearrange("p (t s) -> p t s", t=2)
                                  ).then_inc(rows_done, 1)
            make_hots(0, first_hots(2))
            drain_tile(dve, "dve", 0, 0, copy)
            make_hots(0, hots_of(2, 2))
            with dve.Fori(0, NB - 2) as i:
                work(i)
                start_block(i + 1)
            work(NB - 2)
            start_block(NB - 1)
            work(NB - 1, last=True)

        @block.tensor
        def _(pe):
            def free_bank(i, *what):
                s = FILLS[what][0]
                pe.wait_ge(bank_out[s], out_count(i, what) - 1)
                return bank[s]

            def copied(i, *what):
                s = FILLS[what][0]
                pe.wait_ge(bank_out[s], out_count(i, what))

            def all_copied(i, *what):
                upto = [x for x in ORDER[:ORDER.index(what) + 1] if not left_out(i, x)]
                for s in range(4):
                    copied(i, *[x for x in upto if FILLS[x][0] == s][-1])

            def filled(last, *what):
                last.then_inc(bank_full[FILLS[what][0]], 1)

            def G_slot(i, use):
                s = use % 2
                pe.wait_ge(G_out_act[s], i * on(s, G_USES) + on(s, use) + 1)
                pe.wait_ge(G_out_dve[s], i * on(s, G_USES) + on(s, use) + 1)
                return s

            def G_copied(i, n):
                for s in range(2):
                    pe.wait_ge(G_out_act[s], i * on(s, G_USES) + on(s, n) + 1)
                    pe.wait_ge(G_out_dve[s], i * on(s, G_USES) + on(s, n) + 1)

            pe.sem_inc(hot_free, RING)
            for free in (*rows_read, *G_out_act, *G_out_dve):
                pe.sem_inc(free, 1)
            pe.wait_ge(const_in, 16)

            def pick(i, n):
                f = table_of(n)
                pe.wait_ge(lo_done, f + 1)
                out = bank[pick_bank(i, n)] if ahead(i) else free_bank(i, "pick", n)
                for k in range(RT):
                    hot = n * RT + k
                    pe.wait_ge(hot_made, hot_count(i, hot))
                    nc.tensor.matmul(out[:, :], hi[f][:, k, :], onehot[:, hot % RING, :],
                                     start=(k == 0), stop=False)
                    nc.tensor.matmul(out[:, :], lo[f][:, k, :], onehot[:, hot % RING, :],
                                     start=False, stop=(k == RT - 1)).then_inc(hot_free, 1)

            def turn_tile(i, t):
                pe.wait_ge(rows_in[t], i * (16 * NG) + 16 * NG)
                pe.wait_ge(dense_in[t], i * 16 + 16)
                for n, four in enumerate(FOURS):
                    out = free_bank(i, "tile", t, n)
                    for k, f in enumerate(four):
                        last = nc.tensor.transpose(out[:, k * P:(k + 1) * P], rows[t][:, f, :], ident)
                    filled(last, "tile", t, n)

            def products(i, t, part):
                for n in part:
                    s = G_slot(i, t * G_TILE + n)
                    for k in range(8):
                        at = 4 * (8 * n + k) * NW
                        group = emb[:, t, at:at + 4 * NW]
                        last = nc.tensor.matmul(
                            psG[s][0:USED, k, 0:4 * (NF - 1)], group[:, 0:USED],
                            group.rearrange("d (q f) -> d q f", q=4)[:, :, 1:NF],
                            start=True, stop=True)
                    last.then_inc(G_full[s], 1)

            def one_dense(i, o):
                out = free_bank(i, "one", o)
                nc.tensor.matmul(out[:, :], wd[:, o * P:(o + 1) * P], emb_q[:, DENSE],
                                 start=True, stop=False)

            def work(i, last=False):
                pick(i, 0)
                pick(i, 1)
                turn_tile(i, 0)
                pick(i, 2)
                turn_tile(i, 1)
                pe.wait_ge(rows_done, 2)
                pe.wait_ge(moved, i * KEPT + KEPT)
                for t in range(TILES):
                    all_copied(i, *(("tile", t, LAST) if t else ("pick", 2)))
                    pe.sem_inc(rows_read[t], 1)
                    products(i, t, FIRST)
                    if 1 <= t < TILES - 1:
                        if not last:
                            pick(i, 2 * t + 1)
                            pick(i, 2 * t + 2)
                        turn_tile(i, t + 1)
                        if not last:
                            copied(i, "pick", 2 * t + 1)
                            copied(i, "pick", 2 * t + 2)
                    products(i, t, SECOND)
                pe.wait_ge(weights_in, 6 * 16)
                pe.wait_ge(wd_done, 1)
                one_dense(i, 0)
                G_copied(i, G_TURN)
                for n, banks in enumerate(TURNS):
                    s = G_slot(i, G_TURN + n)
                    for half in range(2):
                        for k, j in enumerate(banks[half]):
                            done = nc.tensor.transpose(psG[s][:, 4 * half + k, 0:USED],
                                                       dots_j[0:USED, j - 1, :],
                                                       ident[0:USED, 0:USED])
                    done.then_inc(G_full[s], 1)
                one_dense(i, 1)
                G_copied(i, G_USES)
                for k in range(PT):
                    out = free_bank(i, "back", k)
                    for q in range(4):
                        done = nc.tensor.transpose(out[0:PW, q * P:(q + 1) * P],
                                                   pairs[:, q, k * PW:(k + 1) * PW], ident)
                    filled(done, "back", k)
                for o in range(O1):
                    if o >= 2:
                        one_dense(i, o)
                    out = bank[FILLS["one", o][0]]
                    for k in range(PT):
                        copied(i, "back", k)
                        done = nc.tensor.matmul(out[:, :], wp[:, k, o * P:(o + 1) * P],
                                                feats[:, k, :], start=False, stop=(k == PT - 1))
                    filled(done, "one", o)
                for q in range(4):
                    out = free_bank(i, "two", q)
                    for k in range(O1):
                        copied(i, "one", k)
                        done = nc.tensor.matmul(out[:, 0:H2], h1[:, k, q * P:(q + 1) * P],
                                                w2_sb[:, k, :], start=(k == 0), stop=(k == O1 - 1))
                    filled(done, "two", q)

            for n in range(SOON, NPICK):
                pick(-1, n)
            with pe.Fori(0, NB - 1) as i:
                work(i)
            work(NB - 1, last=True)


def kernel(**inputs):
    import concourse.bacc as bacc
    from concourse.bass_utils import run_bass_kernel_spmd

    ids = np.asarray(inputs["ids"])
    w1 = np.asarray(inputs["W_top1"])
    batch = ids.shape[0]
    arrays = {f"tbl_{f}": np.ascontiguousarray(inputs[f"tbl_{f}"]) for f in range(TABLES)}
    arrays["ids_g"] = np.ascontiguousarray(ids[:, GATHERED])
    arrays["ids_p"] = np.ascontiguousarray(ids[:, PICKED].T)
    arrays["dense"] = np.ascontiguousarray(inputs["r_dense_features"])
    consts = np.zeros((P, P + RT), np.float32)
    consts[:, :P] = np.eye(P)
    consts[:, P:] = np.arange(P)[:, None] + RW * np.arange(RT)
    arrays["consts"] = consts
    arrays["w_pairs"] = np.ascontiguousarray(w1[pair_rows()])
    arrays["w_dense"] = np.ascontiguousarray(np.stack([w1[:P], w1[P + PAIRS:]]))
    arrays["b1"] = np.ascontiguousarray(np.asarray(inputs["b_top1"]).reshape(-1, P).T)
    arrays["w2"] = np.ascontiguousarray(inputs["W_top2"])
    arrays["last"] = np.concatenate([np.asarray(inputs["b_top2"]),
                                     np.asarray(inputs["W_top3"])[:, 0]])[None, :]

    nc = bacc.Bacc("TRN2", target_bir_lowering=False, num_devices=1)
    ap = {n: nc.dram_tensor(n, a.shape, mybir.dt.from_np(a.dtype), kind="ExternalInput").ap()
          for n, a in arrays.items()}
    y = nc.dram_tensor("y", (1, batch), F32, kind="ExternalOutput").ap()
    build(nc, [ap[f"tbl_{f}"] for f in range(TABLES)], ap["ids_g"], ap["ids_p"], ap["dense"],
          ap["consts"], ap["w_pairs"], ap["w_dense"], ap["b1"], ap["w2"], ap["last"], y)
    result = run_bass_kernel_spmd(nc, [arrays], core_ids=[0])
    return np.asarray(result.results[0]["y"]).reshape(batch, 1)
```

```python
from contextlib import ExitStack

import numpy as np

import concourse.bass as bass
from concourse import mybir

P = 128
TILES = 4
BLK = TILES * P
TABLES = 26
PICKED = [0, 3, 7, 9, 11, 17, 22]
GATHERED = [f for f in range(TABLES) if f not in PICKED]
NPICK = len(PICKED)
NG = len(GATHERED)
NF = TABLES + 1
DENSE = NG
PAIRS = NF * (NF - 1) // 2
PT = 3
PW = PAIRS // PT
ROWS = 1000
RT = 8
RW = ROWS // RT
KEPT = 4
SOON = NPICK - KEPT
RING = 3
WIDE = 2
GROUPS = P // 4
NW = 32
USED = 4 * NW - (NW - NF + 1)

ALU = mybir.AluOpType
ACT = mybir.ActivationFunctionType
F32 = mybir.dt.float32
F32R = mybir.dt.float32r
I32 = mybir.dt.int32


def place_of_feature():
    return [1 + f for f in GATHERED] + [0] + [1 + f for f in PICKED]


def pair_rows():
    feature = place_of_feature()
    rows = []
    for j in range(1, NF):
        for i in range(j):
            a, b = sorted((feature[i], feature[j]))
            rows.append(P + a * NF - a * (a + 1) // 2 + b - a - 1)
    return np.array(rows)


def build(nc, tables, ids_g, ids_p, dense, consts, w_pairs, w_dense, b1, w2, last, y):
    NB = dense.shape[1] // BLK
    H1, H2 = w2.shape
    O1 = H1 // P

    FOURS = [list(range(a, min(a + 4, NG))) for a in range(0, NG, 4)]
    LAST = len(FOURS) - 1

    def tile_fills(t):
        return [("tile", t, n) for n in range(len(FOURS))]

    def picks(*some):
        return [("pick", n) for n in some]

    EARLY = picks(0, 1, 2) + tile_fills(0) + picks(3) + tile_fills(1) + picks(4, 5) + tile_fills(2)
    EARLY += picks(6) + tile_fills(3)
    assert SOON == 3 and KEPT == 4
    FILLS = {what: (n % 4, "dve" if what[0] == "tile" and what[2] % 2 else "act")
             for n, what in enumerate(EARLY)}
    a, b, c, d = [(len(EARLY) + n) % 4 for n in range(4)]
    FILLS |= {("back", 0): (c, "act"), ("back", 1): (d, "dve"),
              ("one", 0): (a, "dve"), ("one", 1): (b, "act"), ("one", 2): (c, "dve"),
              ("one", 3): (d, "act"), ("two", 0): (a, "dve"), ("two", 1): (b, "dve"),
              ("two", 2): (c, "dve"), ("two", 3): (d, "dve")}
    ORDER = list(FILLS)
    assert PT == 3 and O1 == 4 and 2 * P == H2

    def left_out(i, what):
        return isinstance(i, int) and i == NB - 1 and what[0] == "pick" and what[1] >= SOON

    def before(i, what, signalled=False):
        return sum(FILLS[x][0] == FILLS[what][0] and not (signalled and x[0] == "pick")
                   and not left_out(i, x) for x in ORDER[:ORDER.index(what)])

    def in_block(bank, signalled=False):
        return sum(FILLS[x][0] == bank and not (signalled and x[0] == "pick") for x in ORDER)

    def ahead(i):
        return isinstance(i, int) and i == -1

    def pick_bank(i, pick):
        return pick - SOON if ahead(i) else FILLS["pick", pick][0]

    def out_count(i, what):
        return i * in_block(FILLS[what][0]) + before(i, what) + 2

    G_TILE = GROUPS // 8
    TURNS = [[list(range(a, a + 4)), list(range(a + 4, a + 7))] for a in range(1, NF - 5, 7)]
    TURNS += [[[NF - 5, NF - 4, NF - 3], [NF - 2, NF - 1]]]
    assert sum((a + b for a, b in TURNS), []) == list(range(1, NF))
    G_TURN = TILES * G_TILE
    G_BACK = G_TURN + len(TURNS)
    G_USES = G_BACK + 1
    HOTS = NPICK * RT

    def on(s, n):
        return (n + 1 - s) // 2

    AHEAD = KEPT * RT

    def hot_count(i, n):
        return i * HOTS + n + 1 + AHEAD

    def hot_user(n):
        return max([m for m in range(n) if m % RING == n % RING] or
                   [m - HOTS for m in range(HOTS) if m % RING == n % RING])

    def table_of(pick):
        return (pick + KEPT) % NPICK

    def ids_buffer(i, pick):
        return (pick + ahead(i)) % WIDE

    def ids_count(i, pick):
        w = ids_buffer(i, pick)
        if ahead(i):
            return (pick - SOON) // WIDE + 1
        return KEPT // WIDE + i * len(range(w, NPICK, WIDE)) + pick // WIDE + 1

    with ExitStack() as ctx:
        def sb(name, shape, dt=F32):
            return ctx.enter_context(nc.sbuf_tensor(name, shape, dt))

        def psum(name, shape):
            return ctx.enter_context(nc.psum_tensor(name, shape, F32))

        def sem(name):
            return ctx.enter_context(nc.semaphore(name))

        rows = [sb(f"rows{t}", [P, DENSE + 1, P]) for t in range(TILES)]
        emb = sb("emb", [P, TILES, P * NW])
        emb_f = emb[:, :, :].rearrange("d t (s f) -> d f t s", f=NW)
        emb_q = emb[:, :, :].rearrange("d t (g q f) -> d f q t g", q=4, f=NW)
        hi = [sb(f"hi{f}", [RW, RT, P], F32R) for f in range(NPICK)]
        lo = [sb(f"lo{f}", [RW, RT, P], F32R) for f in range(NPICK)]
        onehot = sb("onehot", [RW, RING, BLK], F32R)
        ids_wide = sb("ids_wide", [P, WIDE, BLK], I32)
        idx = [sb(f"idx{t}", [P, NG], I32) for t in range(TILES)]
        dots = sb("dots", [P, (NF - 1) * P])
        dots_j = dots[:, :].rearrange("p (j g) -> p j g", j=NF - 1)
        raw = [dots[0:RW, s * RT * P:(s + 1) * RT * P].rearrange("p (k d) -> p k d", k=RT)
               for s in range(3)]
        raw += [rows[t][0:RW, a:a + RT, :] for t in (2, 3) for a in (0, RT)]
        h1 = dots[:, 0:O1 * BLK].rearrange("p (o s) -> p o s", o=O1)
        pairs = sb("pairs", [P, 4, PAIRS])
        feats_h2 = sb("feats_h2", [P, PT, BLK])
        feats = feats_h2[0:PW, :, :]
        h2 = feats_h2[:, 0, :].rearrange("p (a n) -> p a n", a=2)
        wd_second = feats_h2[:, 1, 0:H1]
        last_in = feats_h2[:, 2, :]
        zeros = feats_h2[:, 0, :]
        b2_row, w3_row = emb_f[:, NF, 0:2, :], emb_f[:, NF + 1, 0:2, :]
        kept = [emb_f[:, NF + 2 + f, :, :].rearrange("d (a b) s -> d a b s", a=2)
                for f in range(KEPT - 1)] + [emb_f[:, NF:NF + 2, 2:TILES, :]]
        assert KEPT == NW - NF - 1 and TILES == 4
        const = sb("const", [P, P + RT])
        ident = const[:, 0:P]
        row_no = const[0:RW, P:P + RT]
        wp = sb("wp", [PW, PT, H1])
        wd = sb("wd", [P, H1])
        w2_sb = sb("w2_sb", [P, O1, H2])
        b1_sb = sb("b1_sb", [P, O1])
        y_sb = sb("y_sb", [P, 4])

        bank = [psum(f"bank{s}", [P, BLK]) for s in range(4)]
        psG = [psum(f"psG{s}", [P, 8, P]) for s in range(2)]

        const_in = sem("const_in")
        weights_in = sem("weights_in")
        raw_in = [sem(f"raw_in{f}") for f in range(NPICK)]
        hi_done, lo_done = sem("hi_done"), sem("lo_done")
        rows_done = sem("rows_done")
        moved = sem("moved")
        dense_placed = sem("dense_placed")
        zeros_made = sem("zeros_made")
        wd_done = sem("wd_done")
        idx_in = [sem(f"idx_in{t}") for t in range(TILES)]
        wide_in = [sem(f"wide_in{w}") for w in range(WIDE)]
        rows_in = [sem(f"rows_in{t}") for t in range(TILES)]
        dense_in = [sem(f"dense_in{t}") for t in range(TILES)]
        rows_read = [sem(f"rows_read{t}") for t in range(TILES)]
        gather_begun = sem("gather_begun")
        hot_made, hot_free = sem("hot_made"), sem("hot_free")
        bank_full = [sem(f"bank_full{s}") for s in range(4)]
        bank_out = [sem(f"bank_out{s}") for s in range(4)]
        G_full = [sem(f"G_full{s}") for s in range(2)]
        G_out_act = [sem(f"G_out_act{s}") for s in range(2)]
        G_out_dve = [sem(f"G_out_dve{s}") for s in range(2)]
        h2_done = sem("h2_done")
        y_out = sem("y_out")

        block = ctx.enter_context(nc.Block())

        def drain(eng, name, i, what, copy, *args):
            s, by = FILLS[what]
            if by == name:
                eng.wait_ge(bank_full[s], i * in_block(s, True) + before(i, what, True) + 1)
                copy(*args).then_inc(bank_out[s], 1)

        def drain_tile(eng, name, i, t, copy):
            for n, four in enumerate(FOURS):
                s = FILLS["tile", t, n][0]
                drain(eng, name, i, ("tile", t, n), copy, emb_f[:, four[0]:four[-1] + 1, t, :],
                      bank[s][:, 0:len(four) * P].rearrange("d (f s) -> d f s", s=P))

        def drain_dots(eng, i, t, part, samples, G_out, copy):
            for n in part:
                use = t * G_TILE + n
                s = use % 2
                g = t * GROUPS + 8 * n
                eng.wait_ge(G_full[s], i * on(s, G_USES) + on(s, use + 1))
                for q in samples:
                    end = min(NW * q + NW, USED)
                    last = copy(dots_j[NW * q:end, :, g:g + 8].rearrange("p j g -> p g j"),
                                psG[s][NW * q:end, :, q * (NF - 1):(q + 1) * (NF - 1)])
                last.then_inc(G_out[s], 1)

        def drain_pairs(eng, i, half, G_out, copy):
            for n, banks in enumerate(TURNS):
                use = G_TURN + n
                s = use % 2
                eng.wait_ge(G_full[s], i * on(s, G_USES) + on(s, use + 1))
                for k, j in enumerate(banks[half]):
                    at = j * (j - 1) // 2
                    last = copy(pairs[:, :, at:at + j],
                                psG[s][:, 4 * half + k, :].rearrange("g (q i) -> g q i", q=4)[:, :, 0:j])
                last.then_inc(G_out[s], 1)

        def drain_feats(eng, name, i, half, G_out, copy):
            for k in range(PT - 1):
                s = FILLS["back", k][0]
                drain(eng, name, i, ("back", k), copy, feats[:, k, :], bank[s][0:PW, :])
            s = G_BACK % 2
            eng.wait_ge(G_full[s], i * on(s, G_USES) + on(s, G_USES))
            at = half * BLK // 2
            copy(feats[:, PT - 1, at:at + BLK // 2],
                 psG[s][0:PW, 4 * half:4 * half + 2, :].rearrange("p q g -> p (q g)")
                 ).then_inc(G_out[s], 1)

        def drain_layers(eng, name, i, relu):
            for o in range(O1):
                s = FILLS["one", o][0]
                drain(eng, name, i, ("one", o), relu, h1[:, o, :], bank[s][:, :], b1_sb[:, o:o + 1])

        KEPT_AT = [(3,), (4, 5), (6,)]
        FIRST, SECOND = range(G_TILE - 1), range(G_TILE - 1, G_TILE)

        @block.sync
        def _(sp):
            def load_idx(i, t):
                sp.dma_start(idx[t][:, :], ids_g[bass.ds(i * BLK + t * P, P), :]
                             ).then_inc(idx_in[t], 16)

            def load_dense(i, t):
                sp.dma_start(rows[t][:, DENSE, :], dense[:, bass.ds(i * BLK + t * P, P)]
                             ).then_inc(dense_in[t], 16)

            load_idx(0, 0)
            for f in range(NPICK):
                sp.dma_start(raw[f], tables[PICKED[f]].rearrange("(p k) d -> p k d", k=RT)
                             ).then_inc(raw_in[f], 16)
                if f % 2:
                    load_dense(0, f // 2)
                    load_idx(0, f // 2 + 1)
            load_dense(0, TILES - 1)
            with sp.Fori(0, NB - 1) as i:
                for t in range(TILES):
                    sp.wait_ge(rows_read[t], i + 2)
                    load_idx(i + 1, t)
                    load_dense(i + 1, t)
            sp.wait_ge(y_out, 16 * (NB + 1))

        @block.gpsimd
        def _(pool):
            with pool.Fori(0, NB) as i:
                for t in range(TILES):
                    pool.wait_ge(idx_in[t], i * 16 + 16)
                    pool.wait_ge(rows_read[t], i + 1)
                    if t >= 2:
                        pool.wait_ge(lo_done, NPICK)
                    pool.sem_inc(gather_begun, 1)
                    for n in range(NG):
                        pool.indirect_dma_start(
                            rows[t][:, n, :], None, tables[GATHERED[n]],
                            bass.IndirectOffsetOnAxis(idx[t][:, n:n + 1], 0)).then_inc(rows_in[t], 16)

        @block.scalar
        def _(act):
            def copy(out, in_):
                return nc.scalar.copy(out, in_)

            def relu(out, in_, bias):
                return nc.scalar.activation(out, in_, ACT.Relu, bias=bias)

            def load_wide(i, pick):
                f, block = table_of(pick), i + (pick >= SOON)
                act.dma_start(ids_wide[:, ids_buffer(i, pick), :],
                              ids_p[f:f + 1, bass.ds(block * BLK, BLK)].to_broadcast([P, BLK])
                              ).then_inc(wide_in[ids_buffer(i, pick)], 16)

            def next_ids(i, pick, last=False):
                act.wait_ge(hot_made, hot_count(i, (pick + 1) * RT - 1))
                if ahead(i) and pick + WIDE >= NPICK:
                    load_wide(0, pick + WIDE - NPICK)
                elif pick + WIDE < (SOON if last else NPICK):
                    load_wide(i, pick + WIDE)
                elif not last:
                    load_wide(i + 1, pick % WIDE)

            def drain_pick(i, pick):
                act.wait_ge(hot_free, hot_count(i, (pick + 1) * RT - 1) + RING)
                s = pick_bank(i, pick)
                if pick < SOON:
                    copy(emb_f[:, DENSE + 1 + table_of(pick), :, :],
                         bank[s][:, :].rearrange("d (t s) -> d t s", t=TILES)
                         ).then_inc(bank_out[s], 1)
                else:
                    copy(kept[pick - SOON], bank[s][:, :].rearrange("d (a b s) -> d a b s", a=2, b=2)
                         ).then_inc(bank_out[s], 1)

            def place_dense(i, t):
                act.wait_ge(dense_in[t], i * 16 + 16)
                copy(emb_f[:, DENSE, t, :], rows[t][:, DENSE, :]).then_inc(dense_placed, 1)

            def move_kept(i):
                for pick in range(SOON, NPICK):
                    s = pick_bank(i, pick)
                    act.wait_ge(bank_out[s], 1 if ahead(i) else out_count(i, ("pick", pick)))
                    copy(emb_f[:, DENSE + 1 + table_of(pick), :, :
                               ].rearrange("d (a b) s -> d a b s", a=2),
                         kept[pick - SOON]).then_inc(moved, 1)

            act.sem_inc(y_out, 16)
            load_wide(-1, SOON)
            act.dma_start(const[:, :], consts).then_inc(const_in, 16)
            load_wide(-1, SOON + 1)
            for f in range(NPICK):
                act.wait_ge(raw_in[f], 16)
                copy(hi[f][:, :, :], raw[f]).then_inc(hi_done, 1)
            loads = [[(wd[:, :], w_dense[0]), (wd_second, w_dense[1]),
                      (last_in, last.to_broadcast([P, 2 * H2])), (b1_sb[:, :], b1)],
                     [(wp[:, :, :], w_pairs.rearrange("(k p) n -> p k n", p=PW))],
                     [(w2_sb[:, :, :], w2.rearrange("(k p) n -> p k n", p=P))], []]
            for pick in range(SOON, NPICK):
                next_ids(-1, pick)
                drain_pick(-1, pick)
                for out, in_ in loads[pick - SOON]:
                    act.dma_start(out, in_).then_inc(weights_in, 16)
            move_kept(-1)
            act.wait_ge(weights_in, 6 * 16)
            for n, row in enumerate((b2_row, w3_row)):
                copy(row, last_in[:, n * H2:(n + 1) * H2].rearrange("p (t s) -> p t s", t=2)
                     ).then_inc(rows_done, 1)

            def work(i, last=False):
                for pick in range(SOON):
                    next_ids(i, pick, last)
                    drain_pick(i, pick)
                place_dense(i, 0)
                drain_tile(act, "act", i, 0, copy)
                if not last:
                    next_ids(i, SOON)
                for t in range(TILES):
                    drain_dots(act, i, t, FIRST, (0, 1), G_out_act, copy)
                    if t < TILES - 1:
                        if not last:
                            for pick in KEPT_AT[t]:
                                if t >= 1:
                                    next_ids(i, pick)
                                drain_pick(i, pick)
                        place_dense(i, t + 1)
                        drain_tile(act, "act", i, t + 1, copy)
                    drain_dots(act, i, t, SECOND, (0, 1), G_out_act, copy)
                drain_pairs(act, i, 0, G_out_act, copy)
                act.wait_ge(y_out, i * 16 + 16)
                drain_feats(act, "act", i, 0, G_out_act, copy)
                act.wait_ge(weights_in, 6 * 16)
                drain_layers(act, "act", i, relu)
                if not last:
                    move_kept(i)
                act.wait_ge(h2_done, i * 4 + 4)
                act.dma_start(y[:, bass.ds(i * BLK, BLK)].rearrange("o (p q) -> (o p) q", q=4),
                              y_sb[:, :]).then_inc(y_out, 16)

            with act.Fori(0, NB - 1) as i:
                work(i)
            work(NB - 1, last=True)

        @block.vector
        def _(dve):
            def add_bias(out, in_):
                return nc.vector.tensor_tensor(out.rearrange("p (t s) -> p t s", t=2),
                                               in_.rearrange("p (t s) -> p t s", t=2), b2_row, ALU.add)

            def copy(out, in_):
                return nc.vector.tensor_copy(out, in_)

            def relu(out, in_, bias):
                return nc.vector.tensor_scalar(out, in_, bias, 0.0, ALU.add, ALU.max)

            def make_lo(f):
                dve.wait_ge(hi_done, f + 1)
                nc.vector.tensor_tensor(lo[f][:, :, :], raw[f], hi[f][:, :, :].bitcast(F32),
                                        ALU.subtract).then_inc(lo_done, 1)

            def make_hots(i, part):
                for n in part:
                    pick, k = divmod(n, RT)
                    if k == 0:
                        dve.wait_ge(wide_in[ids_buffer(i, pick)], ids_count(i, pick) * 16)
                    dve.wait_ge(hot_free, hot_count(i, hot_user(n)) + RING)
                    nc.vector.tensor_scalar(onehot[:, n % RING, :],
                                            ids_wide[0:RW, ids_buffer(i, pick), :],
                                            row_no[:, k:k + 1], None, ALU.is_equal
                                            ).then_inc(hot_made, 1)

            NEXT = 2

            def hots_of(first, last):
                return range(first * RT + RING, (last + 1) * RT)

            def first_hots(pick):
                return range(pick * RT, pick * RT + RING)

            def start_block(i, last=False):
                make_hots(i, range(RING + NEXT, SOON * RT))
                turn_first(i, last)

            def turn_first(i, last=False):
                if not last:
                    make_hots(i, first_hots(SOON))
                drain_tile(dve, "dve", i, 0, copy)
                if not last:
                    make_hots(i, hots_of(SOON, SOON))

            def work(i, last=False):
                for t in range(TILES):
                    if t == 3 and not last:
                        make_hots(i + 1, first_hots(0))
                    drain_dots(dve, i, t, FIRST, (2, 3), G_out_dve, copy)
                    if t < TILES - 1:
                        if t >= 1 and not last:
                            make_hots(i, hots_of(KEPT_AT[t][0], KEPT_AT[t][-1]))
                        drain_tile(dve, "dve", i, t + 1, copy)
                        if t <= 1 and not last:
                            make_hots(i, first_hots(KEPT_AT[t + 1][0]))
                    drain_dots(dve, i, t, SECOND, (2, 3), G_out_dve, copy)
                drain_pairs(dve, i, 1, G_out_dve, copy)
                drain_feats(dve, "dve", i, 1, G_out_dve, copy)
                drain_layers(dve, "dve", i, relu)
                for q in range(4):
                    s = FILLS["two", q][0]
                    drain(dve, "dve", i, ("two", q), add_bias, h2[:, q % 2, :],
                          bank[s][:, 0:H2])
                    dve.wait_ge(bank_out[s], out_count(i, ("two", q)))
                    if q == 3 and not last:
                        make_hots(i + 1, range(RING, RING + NEXT))
                    nc.vector.scalar_tensor_tensor(
                        h2[:, q % 2, :].rearrange("p (t s) -> p t s", t=2),
                        h2[:, q % 2, :].rearrange("p (t s) -> p t s", t=2), 0.0, w3_row,
                        ALU.max, ALU.mult, accum_out=y_sb[:, q:q + 1]).then_inc(h2_done, 1)

            nc.vector.memset(zeros, 0.0).then_inc(zeros_made, 1)
            dve.wait_ge(const_in, 16)
            make_hots(-1, first_hots(SOON))
            make_lo(0)
            for f in range(NPICK):
                if f + 1 < NPICK:
                    make_lo(f + 1)
                i, pick = (-1, SOON + f) if f < KEPT else (0, f - KEPT)
                make_hots(i, range(pick * RT + (RING if f == 0 else 0), (pick + 1) * RT))
            turn_first(0)
            dve.wait_ge(weights_in, 6 * 16)
            nc.vector.tensor_tensor(wd[:, :], wd[:, :], wd_second, ALU.add).then_inc(wd_done, 1)
            with dve.Fori(0, NB - 2) as i:
                work(i)
                start_block(i + 1)
            work(NB - 2)
            start_block(NB - 1, last=True)
            work(NB - 1, last=True)

        @block.tensor
        def _(pe):
            def free_bank(i, *what):
                s = FILLS[what][0]
                pe.wait_ge(bank_out[s], out_count(i, what) - 1)
                return bank[s]

            def copied(i, *what):
                s = FILLS[what][0]
                pe.wait_ge(bank_out[s], out_count(i, what))

            def all_copied(i, *what):
                upto = [x for x in ORDER[:ORDER.index(what) + 1] if not left_out(i, x)]
                for s in range(4):
                    copied(i, *[x for x in upto if FILLS[x][0] == s][-1])

            def filled(last, *what):
                last.then_inc(bank_full[FILLS[what][0]], 1)

            def G_slot(i, use):
                s = use % 2
                pe.wait_ge(G_out_act[s], i * on(s, G_USES) + on(s, use) + 1)
                pe.wait_ge(G_out_dve[s], i * on(s, G_USES) + on(s, use) + 1)
                return s

            def G_copied(i, n):
                for s in range(2):
                    pe.wait_ge(G_out_act[s], i * on(s, G_USES) + on(s, n) + 1)
                    pe.wait_ge(G_out_dve[s], i * on(s, G_USES) + on(s, n) + 1)

            pe.wait_ge(zeros_made, 1)
            for _ in range(5):
                nc.tensor.matmul(bank[3][:, :], zeros[:, 0:P], zeros, start=True, stop=True)
            pe.sem_inc(hot_free, RING)
            for free in (*rows_read, *G_out_act, *G_out_dve):
                pe.sem_inc(free, 1)
            pe.wait_ge(const_in, 16)

            def pick(i, n):
                f = table_of(n)
                pe.wait_ge(lo_done, f + 1)
                out = bank[pick_bank(i, n)] if ahead(i) else free_bank(i, "pick", n)
                for k in range(RT):
                    hot = n * RT + k
                    pe.wait_ge(hot_made, hot_count(i, hot))
                    nc.tensor.matmul(out[:, :], hi[f][:, k, :], onehot[:, hot % RING, :],
                                     start=(k == 0), stop=False)
                    nc.tensor.matmul(out[:, :], lo[f][:, k, :], onehot[:, hot % RING, :],
                                     start=False, stop=(k == RT - 1)).then_inc(hot_free, 1)

            def turn_tile(i, t):
                pe.wait_ge(rows_in[t], i * (16 * NG) + 16 * NG)
                for n, four in enumerate(FOURS):
                    out = free_bank(i, "tile", t, n)
                    for k, f in enumerate(four):
                        last = nc.tensor.transpose(out[:, k * P:(k + 1) * P], rows[t][:, f, :], ident)
                    filled(last, "tile", t, n)

            def products(i, t, part):
                for n in part:
                    s = G_slot(i, t * G_TILE + n)
                    for k in range(8):
                        at = 4 * (8 * n + k) * NW
                        group = emb[:, t, at:at + 4 * NW]
                        last = nc.tensor.matmul(
                            psG[s][0:USED, k, 0:4 * (NF - 1)], group[:, 0:USED],
                            group.rearrange("d (q f) -> d q f", q=4)[:, :, 1:NF],
                            start=True, stop=True)
                    last.then_inc(G_full[s], 1)

            def one_dense(i, o):
                out = free_bank(i, "one", o)
                nc.tensor.matmul(out[:, :], wd[:, o * P:(o + 1) * P], emb_q[:, DENSE],
                                 start=True, stop=False)

            def work(i, last=False):
                for n in range(SOON):
                    pick(i, n)
                pe.wait_ge(rows_done, 2)
                pe.wait_ge(moved, i * KEPT + KEPT)
                turn_tile(i, 0)
                pe.wait_ge(dense_placed, i * TILES + 1)
                if not last:
                    pick(i, SOON)
                for t in range(TILES):
                    all_copied(i, "tile", t, LAST)
                    if t >= 1:
                        pe.wait_ge(dense_placed, i * TILES + t + 1)
                    pe.sem_inc(rows_read[t], 1)
                    products(i, t, FIRST)
                    if t < TILES - 1:
                        if t >= 1 and not last:
                            for n in KEPT_AT[t]:
                                pick(i, n)
                        turn_tile(i, t + 1)
                        if not last:
                            for n in KEPT_AT[t]:
                                copied(i, "pick", n)
                    products(i, t, SECOND)
                pe.wait_ge(weights_in, 6 * 16)
                pe.wait_ge(wd_done, 1)
                one_dense(i, 0)
                G_copied(i, G_TURN)
                for n, banks in enumerate(TURNS):
                    s = G_slot(i, G_TURN + n)
                    for half in range(2):
                        for k, j in enumerate(banks[half]):
                            done = nc.tensor.transpose(psG[s][:, 4 * half + k, 0:USED],
                                                       dots_j[0:USED, j - 1, :],
                                                       ident[0:USED, 0:USED])
                    done.then_inc(G_full[s], 1)
                one_dense(i, 1)
                G_copied(i, G_BACK)
                for k in range(PT):
                    if k < PT - 1:
                        out = free_bank(i, "back", k)[0:PW, :].rearrange("p (q g) -> p q g", q=4)
                    else:
                        out = psG[G_BACK % 2][0:PW, :, :]
                    for q in range(4):
                        at = q if k < PT - 1 else 4 * (q // 2) + q % 2
                        done = nc.tensor.transpose(out[:, at, :], pairs[:, q, k * PW:(k + 1) * PW],
                                                   ident)
                    if k < PT - 1:
                        filled(done, "back", k)
                    else:
                        done.then_inc(G_full[G_BACK % 2], 1)
                for o in range(O1):
                    if o >= 2:
                        one_dense(i, o)
                    out = bank[FILLS["one", o][0]]
                    for k in range(PT):
                        if k < PT - 1:
                            copied(i, "back", k)
                        else:
                            G_copied(i, G_USES)
                        done = nc.tensor.matmul(out[:, :], wp[:, k, o * P:(o + 1) * P],
                                                feats[:, k, :], start=False, stop=(k == PT - 1))
                    filled(done, "one", o)
                for q in range(4):
                    out = free_bank(i, "two", q)
                    for k in range(O1):
                        copied(i, "one", k)
                        done = nc.tensor.matmul(out[:, 0:H2], h1[:, k, q * P:(q + 1) * P],
                                                w2_sb[:, k, :], start=(k == 0), stop=(k == O1 - 1))
                    filled(done, "two", q)

            for n in range(SOON, NPICK):
                pick(-1, n)
            with pe.Fori(0, NB - 1) as i:
                work(i)
            work(NB - 1, last=True)


def kernel(**inputs):
    import concourse.bacc as bacc
    from concourse.bass_utils import run_bass_kernel_spmd

    ids = np.asarray(inputs["ids"])
    w1 = np.asarray(inputs["W_top1"])
    batch = ids.shape[0]
    arrays = {f"tbl_{f}": np.ascontiguousarray(inputs[f"tbl_{f}"]) for f in range(TABLES)}
    arrays["ids_g"] = np.ascontiguousarray(ids[:, GATHERED])
    arrays["ids_p"] = np.ascontiguousarray(ids[:, PICKED].T)
    arrays["dense"] = np.ascontiguousarray(np.asarray(inputs["r_dense_features"]).T)
    consts = np.zeros((P, P + RT), np.float32)
    consts[:, :P] = np.eye(P)
    consts[:, P:] = RT * np.arange(P)[:, None] + np.arange(RT)
    arrays["consts"] = consts
    arrays["w_pairs"] = np.ascontiguousarray(w1[pair_rows()])
    arrays["w_dense"] = np.ascontiguousarray(np.stack([w1[:P], w1[P + PAIRS:]]))
    arrays["b1"] = np.ascontiguousarray(np.asarray(inputs["b_top1"]).reshape(-1, P).T)
    arrays["w2"] = np.ascontiguousarray(inputs["W_top2"])
    arrays["last"] = np.concatenate([np.asarray(inputs["b_top2"]),
                                     np.asarray(inputs["W_top3"])[:, 0]])[None, :]

    nc = bacc.Bacc("TRN2", target_bir_lowering=False, num_devices=1)
    ap = {n: nc.dram_tensor(n, a.shape, mybir.dt.from_np(a.dtype), kind="ExternalInput").ap()
          for n, a in arrays.items()}
    y = nc.dram_tensor("y", (1, batch), F32, kind="ExternalOutput").ap()
    build(nc, [ap[f"tbl_{f}"] for f in range(TABLES)], ap["ids_g"], ap["ids_p"], ap["dense"],
          ap["consts"], ap["w_pairs"], ap["w_dense"], ap["b1"], ap["w2"], ap["last"], y)
    result = run_bass_kernel_spmd(nc, [arrays], core_ids=[0])
    return np.asarray(result.results[0]["y"]).reshape(batch, 1)
```
